# Optimizing a Trainium2 kernel written in Bass

```python
import numpy as np
import jax
import jax.numpy as jnp

def _softmax(x, axis=-1):
    return jax.nn.softmax(x, axis=axis)

def _gelu(x):
    return jax.nn.gelu(x, approximate=True)

def _silu(x):
    return jax.nn.silu(x)

def _sigmoid(x):
    return jax.nn.sigmoid(x)

def _layernorm(x, axis=-1, eps=1e-05):
    m = jnp.mean(x, axis=axis, keepdims=True)
    v = jnp.var(x, axis=axis, keepdims=True)
    return (x - m) / jnp.sqrt(v + eps)

def _scatter_add(tgt, idx, src, axis=0):
    return tgt.at[idx].add(src)

def _segment_sum(src, seg, n):
    return jax.ops.segment_sum(src, seg, n)
kernel_name = 'mk_rec_standalone_d1_rec_r8_42b6b2'

def setup_inputs(seed: int=0):
    np.random.seed(seed)
    _w = jnp.asarray

    def _rec_inputs():
        import jax
        import jax.numpy as jnp
        _rk = jax.random.key(seed)
        r_x = -0.000520686 + 1.00062 * jax.random.normal(jax.random.fold_in(_rk, 1), (2048, 32, 32), jnp.float32)
        return r_x
    r_x = _rec_inputs()

    def _L0_rec_setup():
        import jax, jax.numpy as jnp
        import numpy as np

        def _cin(x, Ws, bs):
            B, F, D = x.shape
            h = x
            directs = []
            n_layers = len(Ws)
            for i, (W, b) in enumerate(zip(Ws, bs)):
                O = W.shape[0]
                H = h.shape[1]
                z = jnp.einsum('bhd,bmd,ohm->bod', h, x, W.reshape(O, H, F))
                z = jax.nn.relu(z + b[None, :, None])
                if i < n_layers - 1:
                    half = O // 2
                    h, direct = (z[:, :half, :], z[:, half:, :])
                else:
                    direct = z
                directs.append(direct)
            out = jnp.concatenate(directs, axis=1)
            return jnp.sum(out, axis=-1)
        key = jax.random.key(seed)
        ks = jax.random.split(key, 4)
        B, F, D = (256, 32, 32)
        x = jax.random.normal(ks[0], (B, F, D), dtype=jnp.float32)
        W0 = jax.random.normal(ks[1], (128, 32 * F), dtype=jnp.float32) * 0.05
        W1 = jax.random.normal(ks[2], (128, 64 * F), dtype=jnp.float32) * 0.05
        W2 = jax.random.normal(ks[3], (1, 64 * F), dtype=jnp.float32) * 0.05
        return {'x': x, 'W0': W0, 'b0': jnp.zeros((128,), jnp.float32), 'W1': W1, 'b1': jnp.zeros((128,), jnp.float32), 'W2': W2, 'b2': jnp.zeros((1,), jnp.float32)}
    _L0_rec_all = _L0_rec_setup()
    _L0_rec_in = {k: v for k, v in _L0_rec_all.items() if k in ('W0', 'b0', 'W1', 'b1', 'W2', 'b2')}
    del _L0_rec_all
    return {'r_x': r_x, 'L0_rec_W0': _L0_rec_in['W0'], 'L0_rec_b0': _L0_rec_in['b0'], 'L0_rec_W1': _L0_rec_in['W1'], 'L0_rec_b1': _L0_rec_in['b1'], 'L0_rec_W2': _L0_rec_in['W2'], 'L0_rec_b2': _L0_rec_in['b2']}

def reference(r_x, L0_rec_W0, L0_rec_b0, L0_rec_W1, L0_rec_b1, L0_rec_W2, L0_rec_b2):
    import jax
    import jax.numpy as jnp

    def _L0_rec_ref(x, W0, b0, W1, b1, W2, b2):
        import jax, jax.numpy as jnp
        import numpy as np

        def _cin(x, Ws, bs):
            B, F, D = x.shape
            h = x
            directs = []
            n_layers = len(Ws)
            for i, (W, b) in enumerate(zip(Ws, bs)):
                O = W.shape[0]
                H = h.shape[1]
                z = jnp.einsum('bhd,bmd,ohm->bod', h, x, W.reshape(O, H, F))
                z = jax.nn.relu(z + b[None, :, None])
                if i < n_layers - 1:
                    half = O // 2
                    h, direct = (z[:, :half, :], z[:, half:, :])
                else:
                    direct = z
                directs.append(direct)
            out = jnp.concatenate(directs, axis=1)
            return jnp.sum(out, axis=-1)
        return _cin(x, (W0, W1, W2), (b0, b1, b2))
    y = _L0_rec_ref(r_x, L0_rec_W0, L0_rec_b0, L0_rec_W1, L0_rec_b1, L0_rec_W2, L0_rec_b2)
    return y

_drawn_inputs = setup_inputs


def setup_inputs(seed=0):
    import zlib

    import numpy as np

    out = dict(_drawn_inputs(seed))
    spreads = {'L0_rec_b0': (0.0, 0.1), 'L0_rec_b1': (0.0, 0.1)}
    factors = {}
    for name, (base, spread) in spreads.items():
        noise = np.random.default_rng([zlib.crc32(name.encode()), seed]).standard_normal(out[name].shape)
        drawn = base * np.exp(spread * noise) if base else spread * noise
        out[name] = jnp.asarray(drawn.astype(out[name].dtype))
    for name, factor in factors.items():
        out[name] = (out[name] * factor).astype(out[name].dtype)
    return out
```

```python
from contextlib import ExitStack

import concourse.bass as bass
from concourse import mybir

F32 = mybir.dt.float32
ALU = mybir.AluOpType
RELU = mybir.ActivationFunctionType.Relu
COPY = mybir.ActivationFunctionType.Copy
AX_X = mybir.AxisListType.X

P = 128
Q = 32
BUFS = 4


def cin_kernel(nc, r_x, W0, b0, W1, b1, W2, b2, out):
    B, F, D = r_x.shape
    O = W0.shape[0]
    H = O // 2
    C = 512
    CB = C // D
    NC = B // CB
    NT = F // 4
    T0 = 4
    CQ = C // 4
    assert F == Q and D == Q and O == P and NC % BUFS == 0 and NC > 2 * BUFS

    with ExitStack() as ctx:
        def sb(name, shape):
            return ctx.enter_context(nc.sbuf_tensor(name, shape, F32))

        def ps(name, shape):
            return ctx.enter_context(nc.psum_tensor(name, shape, F32))

        def sem(name):
            return ctx.enter_context(nc.semaphore(name))

        x4 = sb("x4", [P, BUFS, C])
        xrot = sb("xrot", [P, BUFS, NT, C])
        xq = sb("xq", [P, BUFS, CQ])
        prod0 = sb("prod0", [P, 2, T0, C])
        prod0h = sb("prod0h", [Q, 2, C])
        prod1 = sb("prod1", [P, 4, 4, C])
        ha = sb("ha", [P, 2, C])
        hb = sb("hb", [P, 2, C])
        h2 = sb("h2", [H, 2, C])
        direct = sb("direct", [P, BUFS, C])
        v = sb("v", [P, 2, CQ])
        zlast = sb("zlast", [P, B // 4])
        sums = sb("sums", [P, B])
        outT = sb("outT", [P, B // (4 * P), 4, O + 1])
        prod0flat = prod0[:, :, :, :].rearrange("p a t n -> p (a t n)")
        w0raw = prod0flat[:, 0:F * F]
        w1raw = prod0flat[:, F * F:(F + H) * F]
        wdbl = prod1[:, :, :, :].rearrange("p a t n -> p (a t n)")[:, 0:3 * F * (2 * F + 1)].rearrange(
            "p (n k) -> p n k", n=3)
        w0rot = sb("w0rot", [P, F // 2 + 1, F])
        w1rot = sb("w1rot", [P, 2, F, F])
        w0T = sb("w0T", [P, T0, O])
        w0hT = sb("w0hT", [Q, O])
        w1T = sb("w1T", [P, 2 * NT, O])
        w2s = sb("w2s", [H, F])
        b0s = sb("b0s", [P, 1])
        b1s = sb("b1s", [P, 1])
        b2s = sb("b2s", [P, 1])
        ident = sb("ident", [P, P])
        qsel = sb("qsel", [P, 4])

        z0 = [ps(f"z0_{i}", [P, C]) for i in range(2)]
        z1 = [ps(f"z1_{i}", [P, C]) for i in range(2)]
        u = ps("u", [P, C])
        zT = ps("zT", [P, C])
        tr = [ps(f"tr_{i}", [P, 4, P]) for i in range(2)]

        s_w = sem("weights_in")
        s_cst0 = sem("const_cleared")
        s_cst = sem("const_ready")
        s_prep = sem("weights_step")
        s_wrot = sem("weights_rotated")
        s_tr = sem("weights_transposed")
        s_trc = sem("weights_copied")
        s_slab = sem("slab_written")
        s_x = [sem(f"x_ready{i}") for i in range(BUFS)]
        s_p0 = sem("prod0_ready")
        s_z0 = sem("z0_done")
        s_h = sem("h_ready")
        s_z0r = sem("z0_read")
        s_p1 = sem("prod1_ready")
        s_p1u = sem("prod1_used")
        s_h2 = sem("h2_ready")
        s_z1r = sem("z1_read")
        s_u = sem("u_done")
        s_v = sem("v_ready")
        s_zT = sem("zT_done")
        s_zl = sem("zlast_ready")
        s_sum = sem("sums_ready")
        s_ot = sem("out_transposed")
        s_otc = sem("out_copied")
        s_out = sem("out_written")

        xrows = nc.dram_tensor("x_rows", [2 * F, B * D], F32).ap()
        slab_in = r_x.rearrange("(s b) f d -> s f b d", b=BUFS * CB)

        def slab_rows(i):
            return xrows[:, bass.ds(i * BUFS * C, BUFS * C)].rearrange("f (b d) -> f b d", d=D)

        def windows(cols):
            (row, _), run = cols.ap
            return bass.AP(cols.tensor, cols.offset, [[row, F], [4 * row, NT], run])

        outd = out.rearrange("(g p k) o -> p g k o", p=P, k=4)

        block = ctx.enter_context(nc.Block())

        def chunks(eng, first, step):
            for c in range(first, BUFS):
                step(c, c)
            with eng.Fori(1, NC // BUFS - 1) as i:
                for k in range(BUFS):
                    step(i * BUFS + k, k)
            for c in range(NC - BUFS, NC):
                step(c, c % BUFS)

        def known(c):
            return isinstance(c, int)

        def wait_from(eng, s, c, first, per, value):
            if not known(c) or c >= first:
                eng.wait_ge(s, value)

        @block.sync
        def _(sp):
            sp.dma_start(w0raw, W0).then_inc(s_w, 16)
            sp.dma_start(w1raw, W1).then_inc(s_w, 16)
            sp.dma_start(w2s[:, :], W2.rearrange("a (h m) -> (a h) m", m=F)).then_inc(s_w, 16)
            sp.dma_start(b0s[:, :], b0.rearrange("(o a) -> o a", a=1)).then_inc(s_w, 16)
            sp.dma_start(b1s[:, :], b1.rearrange("(o a) -> o a", a=1)).then_inc(s_w, 16)
            sp.dma_start(b2s[:, :], b2.rearrange("(o a) -> o a", a=1).broadcast_to([P, 1])).then_inc(s_w, 16)

            def copy_slab(i):
                for half in range(2):
                    sp.dma_start(slab_rows(i)[F * half:F * half + F], slab_in[i]).then_inc(s_slab, 16)

            def load(c, k):
                if not known(c) or c >= BUFS:
                    sp.wait_ge(s_v, c - BUFS + 1)
                cols = xrows[0:F, bass.ds(c * C, C)]
                sp.dma_start(x4[:, k, :], cols.unsqueeze(0).broadcast_to([4, F, C])).then_inc(s_x[k], 16)
                for q in range(4):
                    sp.dma_start(xrot[Q * q:Q * q + Q, k, :, :],
                                 windows(xrows[q:q + F, bass.ds(c * C, C)])).then_inc(s_x[k], 16)
                sp.dma_start(xq[:, k, :], cols.rearrange("f (q n) -> q f n", q=4)).then_inc(s_x[k], 16)

            def slab(i, last=False):
                sp.wait_ge(s_slab, 32 * i + 32)
                if not last:
                    copy_slab(i + 1)
                for k in range(BUFS):
                    load(i * BUFS + k, k)

            copy_slab(0)
            slab(0)
            with sp.Fori(1, NC // BUFS - 1) as i:
                slab(i)
            slab(NC // BUFS - 1, last=True)

            sp.wait_ge(s_otc, 2)
            sp.dma_start(outd, outT[:, :, :, :]).then_inc(s_out, 16)
            sp.wait_ge(s_out, 16)

        XDMAS = 6

        @block.gpsimd
        def _(pool):
            nc.gpsimd.memset(ident[:], 0.0).then_inc(s_cst0, 1)
            nc.gpsimd.memset(qsel[:], 0.0).then_inc(s_cst0, 1)
            pool.wait_ge(s_cst0, 2)
            nc.gpsimd.affine_select(out=ident[:], in_=ident[:], compare_op=ALU.not_equal, fill=1.0, base=0,
                                    pattern=[[-1, P]], channel_multiplier=1).then_inc(s_cst, 1)
            for q in range(4):
                pool.wait_ge(s_cst, q + 1)
                nc.gpsimd.memset(qsel[Q * q:Q * q + Q, q:q + 1], 1.0).then_inc(s_cst, 1)

        @block.tensor
        def _(pe):
            pe.wait_ge(s_cst, 5)
            pe.wait_ge(s_wrot, 1)
            for t in range(T0):
                mm = nc.tensor.transpose(tr[0][:, t, :], w0rot[:, 4 * t:4 * t + 4, :].rearrange("o r i -> o (r i)"),
                                         ident[:])
            mm.then_inc(s_tr, 1)
            nc.tensor.transpose(tr[1][0:Q, 0, :], w0rot[:, F // 2, :], ident[:]).then_inc(s_tr, 1)
            pe.wait_ge(s_wrot, 2)
            for g in range(2 * NT // 4):
                pe.wait_ge(s_trc, g + 1)
                for j in range(4):
                    t = 4 * g + j
                    mm = nc.tensor.transpose(tr[g % 2][:, j, :], w1rot[:, t // NT, 4 * (t % NT):4 * (t % NT) + 4, :]
                                             .rearrange("o r i -> o (r i)"), ident[:])
                mm.then_inc(s_tr, 1)
            pe.wait_ge(s_trc, 2 + 2 * NT // 4)

            def layer0(c, k):
                if not known(c) or c >= 2:
                    pe.wait_ge(s_z0r, c - 1)
                pe.wait_ge(s_p0, 2 * c + 1)
                for t in range(T0):
                    nc.tensor.matmul(z0[k % 2][:, :], w0T[:, t, :], prod0[:, k % 2, t, :], start=(t == 0), stop=False)
                if not known(c) or c >= 2:
                    pe.wait_ge(s_h2, c - 1)
                    if not known(c) or c >= 3:
                        pe.wait_ge(s_v, c - 2)
                pe.wait_ge(s_p0, 2 * c + 2)
                nc.tensor.matmul(z0[k % 2][:, :], w0hT[:, :], prod0h[:, k % 2, :], start=False,
                                 stop=True).then_inc(s_z0, 1)

            def layer1(c, k):
                if not known(c) or c >= 2:
                    pe.wait_ge(s_z1r, c - 1)
                for n in range(4):
                    pe.wait_ge(s_p1, 4 * c + n + 1)
                    for j in range(4):
                        t = 4 * n + j
                        mm = nc.tensor.matmul(z1[k % 2][:, :], w1T[:, t, :], prod1[:, n, j, :], start=(t == 0),
                                              stop=(t == 2 * NT - 1))
                    mm.then_inc(s_p1u, 1)

            def layer2_u(c, k):
                for q in range(4):
                    mm = nc.tensor.matmul(u[Q * q:Q * q + Q, 0:CQ], w2s[:, :], h2[:, k % 2, CQ * q:CQ * q + CQ],
                                          start=True, stop=True)
                mm.then_inc(s_u, 1)

            def layer2_sum(c, k):
                pe.wait_ge(s_v, c + 1)
                if not known(c) or c >= 1:
                    pe.wait_ge(s_zl, c)
                nc.tensor.matmul(zT[:, 0:4], v[:, k % 2, :], qsel[:, :], start=True, stop=True).then_inc(s_zT, 1)

            def step(c, k):
                if not known(c) or c + 1 < NC:
                    layer0(c + 1, (k + 1) % BUFS)
                if known(c) and c + 1 == NC:
                    pe.wait_ge(s_h2, c)
                    pe.wait_ge(s_v, c - 1)
                if not known(c) or c >= 1:
                    layer2_u(c - 1, (k - 1) % BUFS)
                layer1(c, k)
                if not known(c) or c >= 1:
                    layer2_sum(c - 1, (k - 1) % BUFS)

            layer0(0, 0)
            chunks(pe, 0, step)
            pe.wait_ge(s_h2, NC)
            pe.wait_ge(s_v, NC - 1)
            layer2_u(NC - 1, (NC - 1) % BUFS)
            layer2_sum(NC - 1, (NC - 1) % BUFS)

            pe.wait_ge(s_sum, NC)
            sv = sums[:, :].rearrange("o (g p k) -> o g k p", p=P, k=4)
            banks = [z0[0], z0[1], z1[0], z1[1]]
            for g in range(B // (4 * P)):
                for k in range(4):
                    mm = nc.tensor.transpose(banks[g][:, P * k:P * k + P], sv[:, g, k, :], ident[:])
            mm.then_inc(s_ot, 1)
            pe.wait_ge(s_zl, NC)
            for g in range(B // (4 * P)):
                mm = nc.tensor.matmul(u[:, 4 * g:4 * g + 4], zlast[:, P * g:P * g + P], qsel[:, :], start=True,
                                      stop=True)
            mm.then_inc(s_ot, 1)

        @block.scalar
        def _(act):
            act.wait_ge(s_w, 16 * 6)
            for n in range(2 + 2 * NT // 4):
                act.wait_ge(s_tr, n + 1)
                if n == 0:
                    cp = nc.scalar.copy(w0T[:, :, :], tr[0][:, :, :])
                elif n == 1:
                    cp = nc.scalar.copy(w0hT[:, :], tr[1][0:Q, 0, :])
                else:
                    cp = nc.scalar.copy(w1T[:, 4 * (n - 2):4 * (n - 2) + 4, :], tr[n % 2][:, :, :])
                cp.then_inc(s_trc, 1)

            def after0(c, k):
                act.wait_ge(s_z0, c + 1)
                if not known(c) or c >= 2:
                    act.wait_ge(s_p1, 4 * c - 4)
                z = z0[k % 2]
                for half in range(2):
                    nc.scalar.activation(ha[H * half:H * half + H, k % 2, :], z[0:H, :], RELU, bias=b0s[0:H, :])
                for q in range(4):
                    s = Q * ((q + 1) % 2)
                    last = nc.scalar.activation(hb[Q * q:Q * q + Q, k % 2, :], z[s:s + Q, :], RELU,
                                                bias=b0s[s:s + Q, :])
                last.then_inc(s_h, 1)
                if not known(c) or c >= BUFS:
                    act.wait_ge(s_sum, c - BUFS + 1)
                nc.scalar.activation(direct[0:H, k, :], z[H:O, :], RELU, bias=b0s[H:O, :]).then_inc(s_z0r, 1)

            def after1(c, k):
                act.wait_ge(s_p1u, 4 * c + 4)
                if not known(c) or c >= 2:
                    act.wait_ge(s_u, c - 1)
                z = z1[k % 2]
                nc.scalar.activation(h2[:, k % 2, :], z[0:H, :], RELU, bias=b1s[0:H, :]).then_inc(s_h2, 1)
                nc.scalar.activation(direct[H:O, k, :], z[H:O, :], RELU, bias=b1s[H:O, :]).then_inc(s_z1r, 1)

            def after2(c, k):
                act.wait_ge(s_zT, c + 1)
                nc.scalar.activation(zlast[:, bass.ds(4 * c, 4)], zT[:, 0:4], RELU, bias=b2s[:, :]).then_inc(s_zl, 1)

            def step(c, k):
                if not known(c) or c + 1 < NC:
                    after0(c + 1, (k + 1) % BUFS)
                if not known(c) or c >= 1:
                    after2(c - 1, (k - 1) % BUFS)
                after1(c, k)

            after0(0, 0)
            chunks(act, 0, step)
            after2(NC - 1, (NC - 1) % BUFS)

            act.wait_ge(s_ot, 2)
            nc.scalar.copy(outT[:, :, :, O:O + 1], u[:, 0:B // P].rearrange("p (g k a) -> p g k a", k=4, a=1)
                           ).then_inc(s_otc, 1)

        @block.vector
        def _(dve):
            dve.wait_ge(s_w, 16 * 6)

            def doubled(n):
                return wdbl[:, n, 0:2 * F * F].rearrange("o (h m) -> o h m", m=2 * F)

            def rotated(n, count):
                return wdbl[:, n, :].rearrange("o (h r) -> o r h", r=2 * F + 1)[:, 0:count, :]

            w0v = w0raw.rearrange("o (h m) -> o h m", m=F)
            for r in range(2):
                nc.vector.tensor_tensor(doubled(0)[:, :, F * r:F * r + F], w0v, w0v.rearrange("o h m -> o m h"),
                                        ALU.add).then_inc(s_prep, 1)
            for n in range(2):
                w1v = w1raw[:, F * F * n:F * F * (n + 1)].rearrange("o (h m) -> o h m", m=F)
                for r in range(2):
                    nc.vector.tensor_copy(doubled(1 + n)[:, :, F * r:F * r + F], w1v).then_inc(s_prep, 1)
            dve.wait_ge(s_prep, 6)
            nc.vector.tensor_copy(w0rot[:, :, :], rotated(0, F // 2 + 1)).then_inc(s_prep, 1)
            dve.wait_ge(s_prep, 7)
            nc.vector.tensor_scalar(w0rot[:, 0:F // 2 + 1:F // 2, :], w0rot[:, 0:F // 2 + 1:F // 2, :], 0.5, None,
                                    ALU.mult).then_inc(s_wrot, 1)
            for ab in range(2):
                for par in range(2):
                    last = nc.vector.tensor_copy(w1rot[:, ab, par::2, :], rotated(1 + (par + ab) % 2, F)[:, par::2, :])
            last.then_inc(s_wrot, 1)

            def layer0(c, k):
                dve.wait_ge(s_x[k], turns(c) * 16 * XDMAS)
                if not known(c) or c >= 2:
                    dve.wait_ge(s_z0, c - 1)
                nc.vector.tensor_tensor(prod0[:, k % 2, :, :], x4[:, k:k + 1, :].broadcast_to([P, T0, C]),
                                        xrot[:, k, 0:T0, :], ALU.mult).then_inc(s_p0, 1)
                nc.vector.tensor_tensor(prod0h[:, k % 2, :], x4[0:Q, k, :], xrot[0:Q, k, T0, :],
                                        ALU.mult).then_inc(s_p0, 1)

            def layer1(c, k):
                dve.wait_ge(s_h, c + 1)
                for n in range(4):
                    if not known(c) or c >= 1:
                        dve.wait_ge(s_p1u, 4 * c + n - 3)
                    hx = ha if n < 2 else hb
                    t = 4 * (n % 2)
                    nc.vector.tensor_tensor(prod1[:, n, :, :], hx[:, k % 2:k % 2 + 1, :].broadcast_to([P, 4, C]),
                                            xrot[:, k, t:t + 4, :], ALU.mult).then_inc(s_p1, 1)

            def layer2(c, k):
                dve.wait_ge(s_u, c + 1)
                if not known(c) or c >= 2:
                    dve.wait_ge(s_zT, c - 1)
                nc.vector.tensor_tensor(v[:, k % 2, :], u[:, 0:CQ], xq[:, k, :], ALU.mult).then_inc(s_v, 1)
                dve.wait_ge(s_z1r, c + 1)
                nc.vector.tensor_reduce(sums[:, bass.ds(c * CB, CB)],
                                        direct[:, k, :].rearrange("o (b d) -> o b d", d=D), AX_X,
                                        ALU.add).then_inc(s_sum, 1)

            index = [None]

            def turns(c):
                return c // BUFS + 1 if known(c) else index[0]

            def step(c, k):
                if not known(c) or c + 1 < NC:
                    layer0(c + 1, (k + 1) % BUFS)
                layer1(c, k)
                if not known(c) or c >= 1:
                    layer2(c - 1, (k - 1) % BUFS)

            layer0(0, 0)
            for c in range(BUFS):
                step(c, c)
            with dve.Fori(1, NC // BUFS - 1) as i:
                for k in range(BUFS):
                    index[0] = i + 1 if k < BUFS - 1 else i + 2
                    step(i * BUFS + k, k)
            for c in range(NC - BUFS, NC):
                step(c, c % BUFS)
            layer2(NC - 1, (NC - 1) % BUFS)

            dve.wait_ge(s_ot, 1)
            for g, bank in enumerate([z0[0], z0[1], z1[0], z1[1]]):
                last = nc.vector.tensor_copy(outT[:, g, :, 0:O], bank[:, :].rearrange("p (k o) -> p k o", k=4))
            last.then_inc(s_otc, 1)


_INS = ['r_x', 'L0_rec_W0', 'L0_rec_b0', 'L0_rec_W1', 'L0_rec_b1', 'L0_rec_W2', 'L0_rec_b2']


def kernel(**inputs):
    import numpy as _np
    import concourse.bacc as _bacc
    from concourse import mybir as _mybir
    from concourse.bass_utils import run_bass_kernel_spmd as _run

    nc = _bacc.Bacc("TRN2", target_bir_lowering=False, num_devices=1)
    arrays, args = {}, []
    for name in _INS:
        a = _np.ascontiguousarray(inputs[name])
        arrays[f"in_{name}_dram"] = a
        args.append(nc.dram_tensor(f"in_{name}_dram", a.shape, _mybir.dt.from_np(a.dtype), kind="ExternalInput").ap())
    shape = (inputs['r_x'].shape[0], inputs['L0_rec_W0'].shape[0] + 1)
    args.append(nc.dram_tensor("out_0_dram", shape, _mybir.dt.float32, kind="ExternalOutput").ap())
    cin_kernel(nc, *args)
    r = _run(nc, [arrays], core_ids=[0])
    return r.results[0]["out_0_dram"]
```

```python
from contextlib import ExitStack

import concourse.bass as bass
from concourse import mybir

F32 = mybir.dt.float32
F32R = mybir.dt.float32r
ALU = mybir.AluOpType
RELU = mybir.ActivationFunctionType.Relu
COPY = mybir.ActivationFunctionType.Copy
AX_X = mybir.AxisListType.X

P = 128
Q = 32
BUFS = 4


def cin_kernel(nc, r_x, W0, b0, W1, b1, W2, b2, out):
    B, F, D = r_x.shape
    O = W0.shape[0]
    H = O // 2
    C = 512
    CB = C // D
    NC = B // CB
    NT = F // 4
    T0 = 4
    CQ = C // 4
    UNITS = [(0, 0, "pool"), (1, 0, "pool"), (0, 4, "dve"), (1, 4, None)]
    NU = len(UNITS)
    NS = sum(how is not None for _, _, how in UNITS)
    MADE = [0, 3, 1, 2]
    TAKEN = [3, 0, 2, 1]
    assert F == Q and D == Q and O == P and NC % BUFS == 0 and NC > 2 * BUFS

    with ExitStack() as ctx:
        def sb(name, shape, dtype=F32):
            return ctx.enter_context(nc.sbuf_tensor(name, shape, dtype))

        def ps(name, shape):
            return ctx.enter_context(nc.psum_tensor(name, shape, F32))

        def sem(name):
            return ctx.enter_context(nc.semaphore(name))

        x4 = sb("x4", [P, BUFS, C])
        xrot = sb("xrot", [P, BUFS, NT, C])
        xq = sb("xq", [P, BUFS, CQ])
        prod0 = sb("prod0", [P, T0, C])
        prod0h = sb("prod0h", [Q, C])
        prod1 = sb("prod1", [P, NU, 4, C])
        prodh = sb("prodh", [P, NS, 4, C], F32R)
        prodl = sb("prodl", [P, NS, 4, C], F32R)
        h2 = sb("h2", [H, 2, C])
        direct = sb("direct", [P, BUFS, C])
        w1rot = direct[:, :, :].rearrange("p b n -> p (b n)").rearrange(
            "p (a r i) -> p a r i", a=2, i=F)
        v = sb("v", [P, 2, CQ])
        zlast = sb("zlast", [P, B // 4])
        sums = sb("sums", [P, B])
        prod1flat = prod1[:, :, :, :].rearrange("p a t n -> p (a t n)")
        w0raw = prod1flat[:, 0:F * F]
        w1raw = prod0[:, :, :].rearrange("p t n -> p (t n)")
        wdbl = prod1flat[:, F * F:F * F + 3 * F * (2 * F + 1)].rearrange("p (n k) -> p n k", n=3)
        outT = prod1flat[:, 0:B // P * (O + 1)].rearrange("p (g k o) -> p g k o", k=4, o=O + 1)
        w0rot = sb("w0rot", [P, F // 2 + 1, F])
        w0T = sb("w0T", [P, T0, O])
        w0hT = sb("w0hT", [Q, O])
        w1T = sb("w1T", [P, NU - NS, 4, O])
        w1Th = sb("w1Th", [P, NS, 4, O], F32R)
        w1Tl = sb("w1Tl", [P, NS, 4, O], F32R)
        w2s = sb("w2s", [H, F])
        b0s = sb("b0s", [P, 1])
        b1s = sb("b1s", [P, 1])
        b2s = sb("b2s", [P, 1])
        ident = sb("ident", [P, P])
        qsel = sb("qsel", [P, 4])

        z0 = ps("z0", [P, C])
        z1 = [ps(f"z1_{i}", [P, C]) for i in range(2)]
        h1 = [[ps(f"h{'ab'[ab]}_{i}", [P, C]) for i in range(2)] for ab in range(2)]
        uz = ps("uz", [P, C])
        u = uz[:, 0:CQ]
        zT = uz[:, CQ:CQ + 4]

        s_w = sem("weights_in")
        s_cst0 = sem("const_cleared")
        s_cst = sem("const_ready")
        s_prep = sem("weights_step")
        s_wrot = sem("weights_rotated")
        s_tr = sem("weights_transposed")
        s_trc = sem("weights_copied")
        s_wl = sem("weights_low")
        s_slab = sem("slab_written")
        s_x = [sem(f"x_ready{i}") for i in range(BUFS)]
        s_p0 = sem("prod0_ready")
        s_z0 = sem("z0_done")
        s_h = sem("h_ready")
        s_z0r = sem("z0_read")
        s_p1 = [sem(f"prod1_ready{n}") for n in range(NU)]
        s_hi = [sem(f"high_ready{n}") for n in range(NS)]
        s_lo = [sem(f"low_ready{n}") for n in range(NS)]
        s_used = [sem(f"prod1_used{n}") for n in range(NU)]
        s_h2 = sem("h2_ready")
        s_z1r = sem("z1_read")
        s_u = sem("u_done")
        s_v = sem("v_ready")
        s_zT = sem("zT_done")
        s_zl = sem("zlast_ready")
        s_sum = sem("sums_ready")
        s_ot = sem("out_transposed")
        s_otc = sem("out_copied")
        s_out = sem("out_written")

        xrows = nc.dram_tensor("x_rows", [2 * F, B * D], F32).ap()
        slab_in = r_x.rearrange("(s b) f d -> s f b d", b=BUFS * CB)

        def slab_rows(i):
            return xrows[:, bass.ds(i * BUFS * C, BUFS * C)].rearrange("f (b d) -> f b d", d=D)

        def windows(cols):
            (row, _), run = cols.ap
            return bass.AP(cols.tensor, cols.offset, [[row, F], [4 * row, NT], run])

        outd = out.rearrange("(g p k) o -> p g k o", p=P, k=4)

        block = ctx.enter_context(nc.Block())

        def chunks(eng, first, step):
            for c in range(first, BUFS):
                step(c, c)
            with eng.Fori(1, NC // BUFS - 1) as i:
                for k in range(BUFS):
                    step(i * BUFS + k, k)
            for c in range(NC - BUFS, NC):
                step(c, c % BUFS)

        def known(c):
            return isinstance(c, int)

        def wait_from(eng, s, c, first, per, value):
            if not known(c) or c >= first:
                eng.wait_ge(s, value)

        def low_half(eng, n, j, count):
            return eng.tensor_tensor(prodl[:, n, j:j + count, :], prod1[:, n, j:j + count, :],
                                     prodh[:, n, j:j + count, :].bitcast(F32), ALU.subtract)

        LOWS = [{"pool": 2, "dve": 1}[how] for _, _, how in UNITS if how]

        @block.sync
        def _(sp):
            sp.dma_start(w0raw, W0).then_inc(s_w, 16)
            sp.dma_start(w1raw, W1).then_inc(s_w, 16)
            sp.dma_start(w2s[:, :], W2.rearrange("a (h m) -> (a h) m", m=F)).then_inc(s_w, 16)
            sp.dma_start(b0s[:, :], b0.rearrange("(o a) -> o a", a=1)).then_inc(s_w, 16)
            sp.dma_start(b1s[:, :], b1.rearrange("(o a) -> o a", a=1)).then_inc(s_w, 16)
            sp.dma_start(b2s[:, :], b2.rearrange("(o a) -> o a", a=1).broadcast_to([P, 1])).then_inc(s_w, 16)

            def copy_slab(i):
                for half in range(2):
                    sp.dma_start(slab_rows(i)[F * half:F * half + F], slab_in[i]).then_inc(s_slab, 16)

            def load(c, k):
                if not known(c) or c >= BUFS:
                    sp.wait_ge(s_v, c - BUFS + 1)
                cols = xrows[0:F, bass.ds(c * C, C)]
                sp.dma_start(x4[:, k, :], cols.unsqueeze(0).broadcast_to([4, F, C])).then_inc(s_x[k], 16)
                for q in range(4):
                    sp.dma_start(xrot[Q * q:Q * q + Q, k, :, :],
                                 windows(xrows[q:q + F, bass.ds(c * C, C)])).then_inc(s_x[k], 16)
                sp.dma_start(xq[:, k, :], cols.rearrange("f (q n) -> q f n", q=4)).then_inc(s_x[k], 16)

            def slab(i, last=False):
                sp.wait_ge(s_slab, 32 * i + 32)
                if not last:
                    copy_slab(i + 1)
                for k in range(BUFS):
                    load(i * BUFS + k, k)

            copy_slab(0)
            slab(0)
            with sp.Fori(1, NC // BUFS - 1) as i:
                slab(i)
            slab(NC // BUFS - 1, last=True)

            sp.wait_ge(s_otc, 2)
            sp.dma_start(outd, outT[:, :, :, :]).then_inc(s_out, 16)
            sp.wait_ge(s_out, 16)

        XDMAS = 6

        @block.gpsimd
        def _(pool):
            nc.gpsimd.memset(ident[:], 0.0).then_inc(s_cst0, 1)
            nc.gpsimd.memset(qsel[:], 0.0).then_inc(s_cst0, 1)
            pool.wait_ge(s_cst0, 2)
            nc.gpsimd.affine_select(out=ident[:], in_=ident[:], compare_op=ALU.not_equal, fill=1.0, base=0,
                                    pattern=[[-1, P]], channel_multiplier=1).then_inc(s_cst, 1)
            for q in range(4):
                pool.wait_ge(s_cst, q + 1)
                nc.gpsimd.memset(qsel[Q * q:Q * q + Q, q:q + 1], 1.0).then_inc(s_cst, 1)

            def step(c, k):
                for n in range(NS):
                    if UNITS[n][2] == "pool":
                        for j in range(2):
                            pool.wait_ge(s_hi[n], 2 * c + j + 1)
                            low_half(nc.gpsimd, n, 2 * j, 2).then_inc(s_lo[n], 1)

            chunks(pool, 0, step)

        @block.tensor
        def _(pe):
            pe.wait_ge(s_cst, 5)
            pe.wait_ge(s_wrot, 1)
            for t in range(T0):
                mm = nc.tensor.transpose(z1[0][:, P * t:P * t + P],
                                         w0rot[:, 4 * t:4 * t + 4, :].rearrange("o r i -> o (r i)"), ident[:])
            mm.then_inc(s_tr, 1)
            nc.tensor.transpose(z1[1][0:Q, 0:P], w0rot[:, F // 2, :], ident[:]).then_inc(s_tr, 1)
            pe.wait_ge(s_wrot, 2)
            for n, (ab, t0, _) in enumerate(UNITS):
                pe.wait_ge(s_trc, n + 1)
                if n >= 2 and n - 2 < NS:
                    pe.wait_ge(s_wl, n - 1)
                for j in range(4):
                    t = t0 + j
                    mm = nc.tensor.transpose(z1[n % 2][:, P * j:P * j + P],
                                             w1rot[:, ab, 4 * t:4 * t + 4, :].rearrange("o r i -> o (r i)"), ident[:])
                mm.then_inc(s_tr, 1)
            pe.wait_ge(s_trc, 2 + NU)
            pe.wait_ge(s_wl, NS)

            def layer0(c, k):
                if not known(c) or c >= 1:
                    pe.wait_ge(s_z0r, c)
                pe.wait_ge(s_p0, 2 * c + 1)
                for t in range(T0):
                    nc.tensor.matmul(z0[:, :], w0T[:, t, :], prod0[:, t, :], start=(t == 0), stop=False)
                pe.wait_ge(s_p0, 2 * c + 2)
                nc.tensor.matmul(z0[:, :], w0hT[:, :], prod0h[:, :], start=False, stop=True).then_inc(s_z0, 1)

            def split_unit(z, n, first, last):
                for j in range(4):
                    for w, p in ((w1Th, prodh), (w1Tl, prodh), (w1Th, prodl)):
                        mm = nc.tensor.matmul(z, w[:, n, j, :], p[:, n, j, :], start=first and j == 0 and w is w1Th
                                              and p is prodh, stop=last and j == 3 and p is prodl)
                mm.then_inc(s_used[n], 1)

            def plain_unit(z, n, first, last):
                for j in range(4):
                    mm = nc.tensor.matmul(z, w1T[:, n - NS, j, :], prod1[:, n, j, :], start=first and j == 0,
                                          stop=last and j == 3)
                mm.then_inc(s_used[n], 1)

            def layer1(c, k):
                if not known(c) or c >= 2:
                    pe.wait_ge(s_z1r, c - 1)
                for m, n in enumerate(TAKEN):
                    if m == 0 and (not known(c) or c >= 1):
                        pe.wait_ge(s_h2, c)
                        if not known(c) or c >= 2:
                            pe.wait_ge(s_zl, c - 1)
                    pe.wait_ge(*((s_lo[n], LOWS[n] * (c + 1)) if n < NS else (s_p1[n], c + 1)))
                    unit = split_unit if n < NS else plain_unit
                    unit(z1[k % 2][:, :], n, m == 0, m == NU - 1)
                    if m == 0 and (not known(c) or c >= 1):
                        layer2_u(c - 1, (k - 1) % BUFS)

            def layer2_u(c, k):
                for q in range(4):
                    mm = nc.tensor.matmul(u[Q * q:Q * q + Q, :], w2s[:, :], h2[:, k % 2, CQ * q:CQ * q + CQ],
                                          start=True, stop=True)
                mm.then_inc(s_u, 1)

            def layer2_sum(c, k):
                pe.wait_ge(s_v, c + 1)
                nc.tensor.matmul(zT, v[:, k % 2, :], qsel[:, :], start=True, stop=True).then_inc(s_zT, 1)

            def step(c, k):
                if not known(c) or c + 1 < NC:
                    layer0(c + 1, (k + 1) % BUFS)
                layer1(c, k)
                if not known(c) or c >= 1:
                    layer2_sum(c - 1, (k - 1) % BUFS)

            layer0(0, 0)
            chunks(pe, 0, step)
            pe.wait_ge(s_h2, NC)
            pe.wait_ge(s_zl, NC - 1)
            layer2_u(NC - 1, (NC - 1) % BUFS)
            layer2_sum(NC - 1, (NC - 1) % BUFS)

            pe.wait_ge(s_sum, NC)
            sv = sums[:, :].rearrange("o (g p k) -> o g k p", p=P, k=4)
            banks = [z1[0], z1[1], h1[0][0], h1[0][1]]
            for g in range(B // (4 * P)):
                for k in range(4):
                    mm = nc.tensor.transpose(banks[g][:, P * k:P * k + P], sv[:, g, k, :], ident[:])
            mm.then_inc(s_ot, 1)
            pe.wait_ge(s_zl, NC)
            for g in range(B // (4 * P)):
                mm = nc.tensor.matmul(uz[:, 4 * g:4 * g + 4], zlast[:, P * g:P * g + P], qsel[:, :], start=True,
                                      stop=True)
            mm.then_inc(s_ot, 1)

        @block.scalar
        def _(act):
            act.wait_ge(s_w, 16 * 6)
            act.wait_ge(s_tr, 1)
            nc.scalar.copy(w0T[:, :, :].rearrange("p t o -> p (t o)"), z1[0][:, :]).then_inc(s_trc, 1)
            act.wait_ge(s_tr, 2)
            nc.scalar.copy(w0hT[:, :], z1[1][0:Q, 0:P]).then_inc(s_trc, 1)
            for n in range(NU):
                act.wait_ge(s_tr, n + 3)
                w = w1Th[:, n, :, :] if n < NS else w1T[:, n - NS, :, :]
                nc.scalar.copy(w.rearrange("p t o -> p (t o)"), z1[n % 2][:, :]).then_inc(s_trc, 1)

            def round_unit(c, n):
                act.wait_ge(s_p1[n], c + 1)
                if not known(c) or c >= 1:
                    act.wait_ge(s_used[n], c)
                for j in range(2):
                    nc.scalar.copy(prodh[:, n, 2 * j:2 * j + 2, :], prod1[:, n, 2 * j:2 * j + 2, :]
                                   ).then_inc(s_hi[n], 1)

            def after0(c, k):
                act.wait_ge(s_z0, c + 1)
                for ab in range(2):
                    if not known(c) or c >= 2:
                        act.wait_ge(s_p1[last_made[ab]], c - 1)
                    if ab == 0:
                        for half in range(2):
                            last = nc.scalar.activation(h1[0][k % 2][H * half:H * half + H, :], z0[0:H, :], RELU,
                                                        bias=b0s[0:H, :])
                    else:
                        for q in range(4):
                            s = Q * ((q + 1) % 2)
                            last = nc.scalar.activation(h1[1][k % 2][Q * q:Q * q + Q, :], z0[s:s + Q, :], RELU,
                                                        bias=b0s[s:s + Q, :])
                    last.then_inc(s_h, 1)
                if not known(c) or c >= BUFS:
                    act.wait_ge(s_sum, c - BUFS + 1)
                nc.scalar.activation(direct[0:H, k, :], z0[H:O, :], RELU, bias=b0s[H:O, :]).then_inc(s_z0r, 1)

            last_made = [[n for n in MADE if UNITS[n][0] == ab][-1] for ab in range(2)]

            def after1(c, k):
                act.wait_ge(s_used[TAKEN[-1]], c + 1)
                if not known(c) or c >= 2:
                    act.wait_ge(s_u, c - 1)
                z = z1[k % 2]
                nc.scalar.activation(h2[:, k % 2, :], z[0:H, :], RELU, bias=b1s[0:H, :]).then_inc(s_h2, 1)
                nc.scalar.activation(direct[H:O, k, :], z[H:O, :], RELU, bias=b1s[H:O, :]).then_inc(s_z1r, 1)

            def after2(c, k):
                act.wait_ge(s_zT, c + 1)
                nc.scalar.activation(zlast[:, bass.ds(4 * c, 4)], zT, RELU, bias=b2s[:, :]).then_inc(s_zl, 1)

            def step(c, k):
                round_unit(c, 0)
                if not known(c) or c >= 1:
                    after1(c - 1, (k - 1) % BUFS)
                if not known(c) or c >= 2:
                    after2(c - 2, (k - 2) % BUFS)
                for n in range(1, NS):
                    round_unit(c, n)
                if not known(c) or c + 1 < NC:
                    after0(c + 1, (k + 1) % BUFS)

            after0(0, 0)
            chunks(act, 0, step)
            after2(NC - 2, (NC - 2) % BUFS)
            after1(NC - 1, (NC - 1) % BUFS)
            after2(NC - 1, (NC - 1) % BUFS)

            act.wait_ge(s_ot, 2)
            nc.scalar.copy(outT[:, :, :, O:O + 1], uz[:, 0:B // P].rearrange("p (g k a) -> p g k a", k=4, a=1)
                           ).then_inc(s_otc, 1)

        @block.vector
        def _(dve):
            dve.wait_ge(s_w, 16 * 6)

            def doubled(n):
                return wdbl[:, n, 0:2 * F * F].rearrange("o (h m) -> o h m", m=2 * F)

            def rotated(n, count):
                return wdbl[:, n, :].rearrange("o (h r) -> o r h", r=2 * F + 1)[:, 0:count, :]

            w0v = w0raw.rearrange("o (h m) -> o h m", m=F)
            for r in range(2):
                nc.vector.tensor_tensor(doubled(0)[:, :, F * r:F * r + F], w0v, w0v.rearrange("o h m -> o m h"),
                                        ALU.add).then_inc(s_prep, 1)
            for n in range(2):
                w1v = w1raw[:, F * F * n:F * F * (n + 1)].rearrange("o (h m) -> o h m", m=F)
                for r in range(2):
                    nc.vector.tensor_copy(doubled(1 + n)[:, :, F * r:F * r + F], w1v).then_inc(s_prep, 1)
            dve.wait_ge(s_prep, 6)
            nc.vector.tensor_copy(w0rot[:, :, :], rotated(0, F // 2 + 1)).then_inc(s_prep, 1)
            dve.wait_ge(s_prep, 7)
            nc.vector.tensor_scalar(w0rot[:, 0:F // 2 + 1:F // 2, :], w0rot[:, 0:F // 2 + 1:F // 2, :], 0.5, None,
                                    ALU.mult).then_inc(s_wrot, 1)
            for ab in range(2):
                for par in range(2):
                    last = nc.vector.tensor_copy(w1rot[:, ab, par::2, :], rotated(1 + (par + ab) % 2, F)[:, par::2, :])
            last.then_inc(s_wrot, 1)
            for n in range(NS):
                dve.wait_ge(s_trc, n + 3)
                nc.vector.tensor_tensor(w1Tl[:, n, :, :].rearrange("p t o -> p (t o)"), z1[n % 2][:, :],
                                        w1Th[:, n, :, :].rearrange("p t o -> p (t o)").bitcast(F32),
                                        ALU.subtract).then_inc(s_wl, 1)

            def layer0(c, k):
                dve.wait_ge(s_x[k], turns(c) * 16 * XDMAS)
                if not known(c) or c >= 1:
                    dve.wait_ge(s_z0, c)
                nc.vector.tensor_tensor(prod0[:, :, :], x4[:, k:k + 1, :].broadcast_to([P, T0, C]),
                                        xrot[:, k, 0:T0, :], ALU.mult).then_inc(s_p0, 1)
                nc.vector.tensor_tensor(prod0h[:, :], x4[0:Q, k, :], xrot[0:Q, k, T0, :], ALU.mult).then_inc(s_p0, 1)

            def layer1(c, k):
                for n in MADE:
                    ab, t0, how = UNITS[n]
                    dve.wait_ge(s_h, 2 * c + ab + 1)
                    if not known(c) or c >= 1:
                        dve.wait_ge(*((s_lo[n], LOWS[n] * c) if how else (s_used[n], c)))
                    nc.vector.tensor_tensor(prod1[:, n, :, :], h1[ab][k % 2][:, :].unsqueeze(1).broadcast_to([P, 4, C]),
                                            xrot[:, k, t0:t0 + 4, :], ALU.mult).then_inc(s_p1[n], 1)
                for n in range(NS):
                    if UNITS[n][2] == "dve":
                        dve.wait_ge(s_hi[n], 2 * c + 2)
                        low_half(nc.vector, n, 0, 4).then_inc(s_lo[n], 1)

            def layer2(c, k):
                dve.wait_ge(s_u, c + 1)
                if not known(c) or c >= 2:
                    dve.wait_ge(s_zT, c - 1)
                nc.vector.tensor_tensor(v[:, k % 2, :], u, xq[:, k, :], ALU.mult).then_inc(s_v, 1)
                dve.wait_ge(s_z1r, c + 1)
                nc.vector.tensor_reduce(sums[:, bass.ds(c * CB, CB)],
                                        direct[:, k, :].rearrange("o (b d) -> o b d", d=D), AX_X,
                                        ALU.add).then_inc(s_sum, 1)

            index = [None]

            def turns(c):
                return c // BUFS + 1 if known(c) else index[0]

            def step(c, k):
                if not known(c) or c + 1 < NC:
                    layer0(c + 1, (k + 1) % BUFS)
                layer1(c, k)
                if not known(c) or c >= 1:
                    layer2(c - 1, (k - 1) % BUFS)

            layer0(0, 0)
            for c in range(BUFS):
                step(c, c)
            with dve.Fori(1, NC // BUFS - 1) as i:
                for k in range(BUFS):
                    index[0] = i + 1 if k < BUFS - 1 else i + 2
                    step(i * BUFS + k, k)
            for c in range(NC - BUFS, NC):
                step(c, c % BUFS)
            layer2(NC - 1, (NC - 1) % BUFS)

            dve.wait_ge(s_ot, 1)
            for g, bank in enumerate([z1[0], z1[1], h1[0][0], h1[0][1]]):
                last = nc.vector.tensor_copy(outT[:, g, :, 0:O], bank[:, :].rearrange("p (k o) -> p k o", k=4))
            last.then_inc(s_otc, 1)


_INS = ['r_x', 'L0_rec_W0', 'L0_rec_b0', 'L0_rec_W1', 'L0_rec_b1', 'L0_rec_W2', 'L0_rec_b2']


def kernel(**inputs):
    import numpy as _np
    import concourse.bacc as _bacc
    from concourse import mybir as _mybir
    from concourse.bass_utils import run_bass_kernel_spmd as _run

    nc = _bacc.Bacc("TRN2", target_bir_lowering=False, num_devices=1)
    arrays, args = {}, []
    for name in _INS:
        a = _np.ascontiguousarray(inputs[name])
        arrays[f"in_{name}_dram"] = a
        args.append(nc.dram_tensor(f"in_{name}_dram", a.shape, _mybir.dt.from_np(a.dtype), kind="ExternalInput").ap())
    shape = (inputs['r_x'].shape[0], inputs['L0_rec_W0'].shape[0] + 1)
    args.append(nc.dram_tensor("out_0_dram", shape, _mybir.dt.float32, kind="ExternalOutput").ap())
    cin_kernel(nc, *args)
    r = _run(nc, [arrays], core_ids=[0])
    return r.results[0]["out_0_dram"]
```

```python
from contextlib import ExitStack

import concourse.bass as bass
from concourse import mybir

F32 = mybir.dt.float32
F32R = mybir.dt.float32r
ALU = mybir.AluOpType
RELU = mybir.ActivationFunctionType.Relu
AX_X = mybir.AxisListType.X

P = 128
Q = 32
BUFS = 4


def cin_kernel(nc, r_x, W0, b0, W1, b1, W2, b2, out):
    B, F, D = r_x.shape
    O = W0.shape[0]
    H = O // 2
    C = 512
    CB = C // D
    NC = B // CB
    NT = F // 4
    HI_LAG = 2
    XQ_LAG = 4
    G = 16
    T0 = 4
    CQ = C // 4
    UNITS = [(0, 0, 4, "pool"), (1, 0, 4, "pool"), (0, 4, 4, "dve"), (1, 4, 2, "pool"), (1, 6, 2, "pool")]
    NU = len(UNITS)
    FIRST = [sum(u[2] for u in UNITS[:n]) for n in range(NU + 1)]
    MADE = [0, 2, 1, 3, 4]
    TAKEN = [0, 2, 1, 3, 4]

    def tiles(n):
        return slice(FIRST[n], FIRST[n + 1])

    def parts(n):
        return [slice(t, t + 2) for t in range(FIRST[n], FIRST[n + 1], 2)]

    assert F == Q and D == Q and O == P and NC % BUFS == 0 and NC > 2 * BUFS

    with ExitStack() as ctx:
        def sb(name, shape, dtype=F32):
            return ctx.enter_context(nc.sbuf_tensor(name, shape, dtype))

        def ps(name, shape):
            return ctx.enter_context(nc.psum_tensor(name, shape, F32))

        def sem(name):
            return ctx.enter_context(nc.semaphore(name))

        x4 = sb("x4", [P, C])
        xlo = sb("xlo", [P, BUFS, T0, C])
        xhi = sb("xhi", [P, 2, NT - T0, C])
        xq = sb("xq", [P, 2, CQ])
        prod0 = sb("prod0", [P, T0, C])
        xa = sb("xa", [P, C])
        xb = sb("xb", [P, C])
        prod16 = sb("prod16", [P, C])
        prod16r = sb("prod16r", [P, C], F32R)
        prod1 = sb("prod1", [P, 2 * NT, C])
        prodh = sb("prodh", [P, 2 * NT, C], F32R)
        prodl = sb("prodl", [P, 2 * NT, C], F32R)
        h2 = sb("h2", [P, C // 2])
        direct = sb("direct", [P, BUFS, C])
        v = sb("v", [P, CQ])
        zlast = sb("zlast", [P, B // 4])
        sums = sb("sums", [P, B])
        prod1flat = prod1[:, :, :].rearrange("p t n -> p (t n)")
        RAW = F * F + 3 * F * (2 * F + 1)
        w0raw = prod1flat[:, 0:F * F]
        w1raw = prod0[:, :, :].rearrange("p t n -> p (t n)")
        wdbl = prod1flat[:, F * F:RAW].rearrange("p (n k) -> p n k", n=3)
        w16flat = prod1flat[:, 0:BUFS * (P + G)]
        w16 = w16flat.rearrange("p (k s) -> p k s", s=P + G)
        outT = prod1flat[:, 0:B // P * (O + 1)].rearrange("p (g k o) -> p g k o", k=4, o=O + 1)
        w1rot = sums[:, 0:2 * F * F].rearrange("p (a r i) -> p a r i", a=2, i=F)
        w0rot = prod1flat[:, RAW:RAW + (F // 2 + 1) * F].rearrange("p (r i) -> p r i", i=F)
        w0T = sb("w0T", [P, T0, O])
        w16h = sb("w16h", [P, BUFS, O], F32R)
        w16l = sb("w16l", [P, BUFS, O], F32R)
        w1Th = sb("w1Th", [P, 2 * NT, O], F32R)
        w1Tl = sb("w1Tl", [P, 2 * NT, O], F32R)
        w2s = sb("w2s", [P, 2 * F])
        small = sb("biases_and_qsel", [P, 7])
        b0s, b1s, b2s = (small[:, n:n + 1] for n in range(3))
        ident = sb("ident", [P, P])
        qsel = small[:, 3:7]

        z0 = ps("z0", [P, C])
        z1 = [ps(f"z1_{i}", [P, C]) for i in range(2)]
        h1 = [[ps("ha_0", [P, C]), ps("ha_1", [P, C])], [ps("hb", [P, C])] * 2]
        xps = ps("xps", [P, C])
        uz = ps("uz", [P, C])
        u = uz[:, 0:CQ]
        zT = uz[:, CQ:CQ + 4]

        s_w0 = sem("w0_in")
        s_w1 = sem("w1_in")
        s_w = sem("small_weights_in")
        s_w1d = sem("w1_doubled")
        s_first = sem("chunk0_written")
        s_cst0 = sem("const_cleared")
        s_cst = sem("const_ready")
        s_prep = sem("weights_step")
        s_wrot = sem("weights_rotated")
        s_tr = sem("weights_transposed")
        s_trc = sem("weights_copied")
        s_wl = sem("weights_low")
        s_slab = sem("slab_written")
        s_x = [sem(f"x_ready{i}") for i in range(BUFS)]
        s_xq = [sem(f"xq_ready{i}") for i in range(2)]
        s_xhi = [sem(f"x_upper_ready{i}") for i in range(2)]
        s_xps = sem("x_in_psum")
        s_p0 = sem("prod0_ready")
        s_x16 = sem("x_pairs_ready")
        s_p16 = sem("prod16_ready")
        s_h16 = sem("prod16_high_ready")
        s_l16 = sem("prod16_low_ready")
        s_z0 = sem("z0_done")
        s_h = sem("h_ready")
        s_z0r = sem("z0_read")
        s_p1 = [sem(f"prod1_ready{n}") for n in range(NU)]
        s_hi = [sem(f"high_ready{n}") for n in range(NU)]
        s_lo = [sem(f"low_ready{n}") for n in range(NU)]
        s_used = [sem(f"prod1_used{n}") for n in range(NU)]
        s_h2 = sem("h2_ready")
        s_z1r = sem("z1_read")
        s_u = sem("u_done")
        s_v = sem("v_ready")
        s_zT = sem("zT_done")
        s_zl = sem("zlast_ready")
        s_sum = sem("sums_ready")
        s_ot = sem("out_transposed")
        s_otc = sem("out_copied")
        s_out = sem("out_written")

        xrows = nc.dram_tensor("x_rows", [2 * F, B * D], F32).ap()
        slab_in = r_x.rearrange("(s b) f d -> s f b d", b=BUFS * CB)

        def slab_rows(i):
            return xrows[:, bass.ds(i * BUFS * C, BUFS * C)].rearrange("f (b d) -> f b d", d=D)

        def windows(cols):
            (row, _), run = cols.ap
            return bass.AP(cols.tensor, cols.offset, [[row, F], [4 * row, T0], run])

        def rotated_x(k, t0, count):
            return xlo[:, k, t0:t0 + count, :] if t0 < T0 else xhi[:, k % 2, t0 - T0:t0 - T0 + count, :]

        outd = out.rearrange("(g p k) o -> p g k o", p=P, k=4)

        block = ctx.enter_context(nc.Block())

        def chunks(eng, step):
            for k in range(BUFS):
                step(0, k)
            with eng.Fori(1, NC // BUFS - 1) as i:
                for k in range(BUFS):
                    step(i, k)
            for k in range(BUFS):
                step(NC // BUFS - 1, k)

        def known(c):
            return isinstance(c, int)

        def w1v(n):
            return w1raw[:, F * F * n:F * F * (n + 1)].rearrange("o (h m) -> o h m", m=F)

        def doubled(n):
            return wdbl[:, n, 0:2 * F * F].rearrange("o (h m) -> o h m", m=2 * F)

        def rotated(n, count):
            return wdbl[:, n, :].rearrange("o (h r) -> o r h", r=2 * F + 1)[:, 0:count, :]

        def low_half(eng, part):
            return eng.tensor_tensor(prodl[:, part, :], prod1[:, part, :], prodh[:, part, :].bitcast(F32),
                                     ALU.subtract)

        LOWS = [len(parts(n)) if UNITS[n][3] == "pool" else 1 for n in range(NU)]

        @block.sync
        def _(sp):
            def copy_slab(i):
                for half in range(2):
                    sp.dma_start(slab_rows(i)[F * half:F * half + F], slab_in[i]).then_inc(s_slab, 16)

            def copy_samples(a, b, done):
                for half in range(2):
                    sp.dma_start(slab_rows(0)[F * half:F * half + F, a:b], slab_in[0][:, a:b]).then_inc(done, 16)

            def load(c, k):
                if not known(c) or c >= BUFS:
                    sp.wait_ge(s_xps, c)
                if not known(c) or c >= HI_LAG:
                    load_hi(c - HI_LAG, (k - HI_LAG) % 2)
                if k == 0 and (not known(c) or c >= BUFS):
                    load_pairs(c)
                for q in range(4):
                    sp.dma_start(xlo[Q * q:Q * q + Q, k, :, :],
                                 windows(xrows[q:q + F, bass.ds(c * C, C)])).then_inc(s_x[k], 16)
                if known(c) and 1 <= c < BUFS:
                    sp.wait_ge(s_xps, c)
                cols = xrows[0:F, bass.ds(c * C, C)]
                sp.dma_start(x4[:, :], cols.unsqueeze(0).broadcast_to([4, F, C])).then_inc(s_x[k], 16)
                if not known(c) or c >= XQ_LAG:
                    load_xq(c - XQ_LAG, (k - XQ_LAG) % 2)

            def load_hi(c, k):
                for q in range(4):
                    sp.dma_start(xhi[Q * q:Q * q + Q, k, :, :],
                                 windows(xrows[4 * T0 + q:4 * T0 + q + F, bass.ds(c * C, C)])).then_inc(s_xhi[k], 16)

            def load_pairs(c):
                for dst, row in ((xa, 0), (xb, G)):
                    src = xrows[row:row + G, bass.ds(c * C, BUFS * C)].rearrange("i (k n) -> k i n", n=C)
                    for half in range(2):
                        sp.dma_start(dst[P // 2 * half:P // 2 * half + P // 2, :], src).then_inc(s_x16, 16)

            def load_xq(c, k):
                cols = xrows[0:F, bass.ds(c * C, C)].rearrange("f (a j n) -> j a f n", a=2, j=2)
                for j in range(2):
                    sp.dma_start(xq[2 * Q * j:2 * Q * j + 2 * Q, k, :], cols[j]).then_inc(s_xq[k], 16)

            def slab(i, last=False):
                sp.wait_ge(s_slab, 32 * i + 32)
                if not last:
                    copy_slab(i + 1)
                for k in range(BUFS):
                    load(i * BUFS + k, k)

            copy_samples(0, CB, s_first)
            sp.wait_ge(s_first, 32)
            load(0, 0)
            copy_samples(CB, BUFS * CB, s_slab)
            sp.wait_ge(s_slab, 32)
            load_pairs(0)
            for k in range(1, BUFS):
                load(k, k)
            copy_slab(1)
            with sp.Fori(1, NC // BUFS - 1) as i:
                slab(i)
            slab(NC // BUFS - 1, last=True)
            sp.wait_ge(s_xps, NC)
            load_hi(NC - 2, 0)
            sp.wait_ge(s_p1[MADE[-1]], NC - 2)
            load_hi(NC - 1, 1)
            for c in range(NC - XQ_LAG, NC):
                sp.wait_ge(s_v, c - 1)
                load_xq(c, c % 2)

            sp.wait_ge(s_otc, 2)
            sp.dma_start(outd, outT[:, :, :, :]).then_inc(s_out, 16)
            sp.wait_ge(s_out, 16)

        XDMAS = 5

        @block.gpsimd
        def _(pool):
            nc.gpsimd.memset(w2s[:], 0.0).then_inc(s_cst, 1)
            nc.gpsimd.memset(ident[:], 0.0).then_inc(s_cst0, 1)
            nc.gpsimd.memset(qsel, 0.0).then_inc(s_cst0, 1)
            pool.wait_ge(s_cst0, 2)
            nc.gpsimd.affine_select(out=ident[:], in_=ident[:], compare_op=ALU.not_equal, fill=1.0, base=0,
                                    pattern=[[-1, P]], channel_multiplier=1).then_inc(s_cst, 1)
            for q in range(4):
                pool.wait_ge(s_cst, q + 2)
                nc.gpsimd.memset(qsel[Q * q:Q * q + Q, q:q + 1], 1.0).then_inc(s_cst, 1)

            def step(i, k):
                c = BUFS * i + k
                for n in MADE:
                    if UNITS[n][3] == "pool":
                        for j, part in enumerate(parts(n)):
                            pool.wait_ge(s_hi[n], LOWS[n] * c + j + 1)
                            low_half(nc.gpsimd, part).then_inc(s_lo[n], 1)

            chunks(pool, step)

        ORDER = [(ab, t0 + j) for ab, t0, count, _ in UNITS for j in range(count)]
        GROUPS = 2 * NT // 4

        def z1_tiles(g, a, b):
            return z1[g % 2][:, P * a:P * b].rearrange("p (t o) -> p t o", o=O)

        @block.tensor
        def _(pe):
            pe.wait_ge(s_cst, 6)
            pe.wait_ge(s_wrot, 1)
            for t in range(T0):
                mm = nc.tensor.transpose(z1[0][:, P * t:P * t + P],
                                         w0rot[:, 4 * t:4 * t + 4, :].rearrange("o r i -> o (r i)"), ident[:])
            mm.then_inc(s_tr, 1)
            for k in range(BUFS):
                mm = nc.tensor.transpose(z1[1][:, P * k:P * k + P], w16flat[:, P * k:P * k + P], ident[:])
            mm.then_inc(s_tr, 1)
            pe.wait_ge(s_wrot, 2)
            for g in range(GROUPS):
                pe.wait_ge(s_trc, g + 1)
                if g >= 1:
                    pe.wait_ge(s_wl, g)
                for j in range(4):
                    ab, t = ORDER[4 * g + j]
                    mm = nc.tensor.transpose(z1[g % 2][:, P * j:P * j + P],
                                             w1rot[:, ab, 4 * t:4 * t + 4, :].rearrange("o r i -> o (r i)"), ident[:])
                mm.then_inc(s_tr, 1)
            pe.wait_ge(s_trc, 2 + GROUPS)
            pe.wait_ge(s_wl, GROUPS + 1)

            def layer0(c, k, i):
                if not known(c) or c >= 1:
                    pe.wait_ge(s_z0r, c)
                pe.wait_ge(s_p0, c + 1)
                for t in range(T0):
                    nc.tensor.matmul(z0[:, :], w0T[:, t, :], prod0[:, t, :], start=(t == 0), stop=False)
                pe.wait_ge(s_l16, i + 1)
                nc.tensor.matmul(z0[:, :], w16h[:, k, :], prod16r[:, :], start=False, stop=False)
                nc.tensor.matmul(z0[:, :], w16l[0:P // 2, k, :], prod16r[0:P // 2, :], start=False,
                                 stop=True).then_inc(s_z0, 1)

            def unit(z, n, first, last):
                for t in range(FIRST[n], FIRST[n + 1]):
                    passes = ((w1Th[:, t, :], prodh[:, t, :]), (w1Th[:, t, :], prodl[:, t, :]),
                              (w1Tl[:, t, :], prodh[:, t, :]))
                    for m, (w, p) in enumerate(passes):
                        mm = nc.tensor.matmul(z, w, p, start=first and t == FIRST[n] and m == 0,
                                              stop=last and t == FIRST[n + 1] - 1 and m == len(passes) - 1)
                mm.then_inc(s_used[n], 1)

            def layer1(c, k, i):
                if not known(c) or c >= 2:
                    pe.wait_ge(s_z1r, c - 1)
                for m, n in enumerate(TAKEN):
                    pe.wait_ge(s_lo[n], LOWS[n] * (c + 1))
                    unit(z1[k % 2][:, :], n, m == 0, m == NU - 1)
                    if m == 0 and (not known(c) or c >= 2):
                        layer2_sum(c - 2, (k - 2) % BUFS)
                    if m == 1 and (not known(c) or c + 2 < NC):
                        layer0(c + 2, (k + 2) % BUFS, i + (k + 2) // BUFS)
                    if m == NU - 2 and (not known(c) or c >= 1):
                        layer2_u(c - 1, (k - 1) % BUFS)

            def layer2_u(c, k):
                pe.wait_ge(s_h2, c + 1)
                if not known(c) or c >= 1:
                    pe.wait_ge(s_zl, c)
                for j in range(2):
                    mm = nc.tensor.matmul(u[H * j:H * j + H, :], w2s[:, :], h2[:, CQ * j:CQ * j + CQ],
                                          start=True, stop=True)
                mm.then_inc(s_u, 1)

            def layer2_sum(c, k):
                pe.wait_ge(s_v, c + 1)
                nc.tensor.matmul(zT, v[:, :], qsel[:, :], start=True, stop=True).then_inc(s_zT, 1)

            layer0(0, 0, 0)
            layer0(1, 1, 0)
            chunks(pe, lambda i, k: layer1(BUFS * i + k, k, i))
            layer2_sum(NC - 2, (NC - 2) % BUFS)
            layer2_u(NC - 1, (NC - 1) % BUFS)
            layer2_sum(NC - 1, (NC - 1) % BUFS)

            pe.wait_ge(s_sum, NC)
            sv = sums[:, :].rearrange("o (g p k) -> o g k p", p=P, k=4)
            banks = [z1[0], z1[1], h1[0][0], h1[0][1]]
            for g in range(B // (4 * P)):
                for k in range(4):
                    mm = nc.tensor.transpose(banks[g][:, P * k:P * k + P], sv[:, g, k, :], ident[:])
            mm.then_inc(s_ot, 1)
            pe.wait_ge(s_zl, NC)
            for g in range(B // (4 * P)):
                mm = nc.tensor.matmul(uz[:, 4 * g:4 * g + 4], zlast[:, P * g:P * g + P], qsel[:, :], start=True,
                                      stop=True)
            mm.then_inc(s_ot, 1)

        @block.scalar
        def _(act):
            def copy_x(c, k, i):
                act.wait_ge(s_x[k], 16 * XDMAS * (i + 1))
                if not known(c) or c >= 1:
                    act.wait_ge(s_p0, c)
                nc.scalar.copy(xps[:, :], x4[:, :]).then_inc(s_xps, 1)

            act.dma_start(w0raw, W0).then_inc(s_w0, 16)
            act.dma_start(w1raw, W1).then_inc(s_w1, 16)
            act.dma_start(b0s[:, :], b0.rearrange("(o a) -> o a", a=1)).then_inc(s_w, 16)
            act.wait_ge(s_cst, 1)
            for half in range(2):
                act.dma_start(w2s[H * half:H * half + H, F * half:F * half + F],
                              W2.rearrange("a (h m) -> (a h) m", m=F)).then_inc(s_w, 16)
            act.dma_start(b1s[:, :], b1.rearrange("(o a) -> o a", a=1)).then_inc(s_w, 16)
            act.dma_start(b2s[:, :], b2.rearrange("(o a) -> o a", a=1).broadcast_to([P, 1])).then_inc(s_w, 16)
            act.wait_ge(s_w1, 16)
            for r in range(2):
                nc.scalar.copy(doubled(2)[:, :, F * r:F * r + F], w1v(1)).then_inc(s_w1d, 1)
            act.wait_ge(s_tr, 1)
            nc.scalar.copy(w0T[:, :, :].rearrange("p t o -> p (t o)"), z1[0][:, :]).then_inc(s_trc, 1)
            act.wait_ge(s_tr, 2)
            nc.scalar.copy(w16h[:, :, :], z1_tiles(1, 0, BUFS)).then_inc(s_trc, 1)
            copy_x(0, 0, 0)
            for g in range(GROUPS):
                act.wait_ge(s_tr, g + 3)
                nc.scalar.copy(w1Th[:, 4 * g:4 * g + 4, :], z1_tiles(g, 0, 4)).then_inc(s_trc, 1)

            def round_unit(c, n):
                act.wait_ge(s_p1[n], c + 1)
                if not known(c) or c >= 1:
                    act.wait_ge(s_used[n], c)
                for part in parts(n):
                    nc.scalar.copy(prodh[:, part, :], prod1[:, part, :]).then_inc(s_hi[n], 1)

            def after0(c, k):
                act.wait_ge(s_z0, c + 1)
                for ab in range(2):
                    back = 2 - ab
                    if not known(c) or c >= back:
                        act.wait_ge(s_p1[last_made[ab]], c - back + 1)
                    if ab == 0:
                        for half in range(2):
                            last = nc.scalar.activation(h1[0][k % 2][H * half:H * half + H, :], z0[0:H, :], RELU,
                                                        bias=b0s[0:H, :])
                    else:
                        for q in range(4):
                            s = Q * ((q + 1) % 2)
                            last = nc.scalar.activation(h1[1][k % 2][Q * q:Q * q + Q, :], z0[s:s + Q, :], RELU,
                                                        bias=b0s[s:s + Q, :])
                    last.then_inc(s_h, 1)
                if not known(c) or c >= BUFS:
                    act.wait_ge(s_sum, c - BUFS + 1)
                nc.scalar.activation(direct[0:H, k, :], z0[H:O, :], RELU, bias=b0s[H:O, :]).then_inc(s_z0r, 1)

            def round16(g):
                act.wait_ge(s_p16, g + 1)
                if not known(g) or g >= 1:
                    act.wait_ge(s_z0, g * BUFS)
                nc.scalar.copy(prod16r[:, :], prod16[:, :]).then_inc(s_h16, 1)

            last_made = [[n for n in MADE if UNITS[n][0] == ab][-1] for ab in range(2)]

            def after1(c, k):
                act.wait_ge(s_used[TAKEN[-1]], c + 1)
                if not known(c) or c >= 1:
                    act.wait_ge(s_u, c)
                z = z1[k % 2]
                for half in range(2):
                    last = nc.scalar.activation(h2[H * half:H * half + H, :],
                                                z[0:H, C // 2 * half:C // 2 * (half + 1)], RELU, bias=b1s[0:H, :])
                last.then_inc(s_h2, 1)
                nc.scalar.activation(direct[H:O, k, :], z[H:O, :], RELU, bias=b1s[H:O, :]).then_inc(s_z1r, 1)

            def after2(c, k):
                act.wait_ge(s_zT, c + 1)
                nc.scalar.activation(zlast[:, bass.ds(4 * c, 4)].rearrange("p (a j) -> p j a", a=2),
                                     zT.rearrange("p (j a) -> p j a", a=2), RELU, bias=b2s[:, :]).then_inc(s_zl, 1)

            def step(i, k):
                c = BUFS * i + k
                round_unit(c, MADE[0])
                if not known(c) or c >= 3:
                    after2(c - 3, (k - 3) % BUFS)
                round_unit(c, MADE[1])
                if not known(c) or c + 2 < NC:
                    copy_x(c + 2, (k + 2) % BUFS, i + (k + 2) // BUFS)
                if k == BUFS - 2 and (not known(c) or c + BUFS < NC):
                    round16(i + 1)
                round_unit(c, MADE[2])
                if not known(c) or c + 1 < NC:
                    after0(c + 1, (k + 1) % BUFS)
                round_unit(c, MADE[3])
                round_unit(c, MADE[4])
                if not known(c) or c >= 1:
                    after1(c - 1, (k - 1) % BUFS)

            act.wait_ge(s_w, 16 * 5)
            round16(0)
            copy_x(1, 1, 0)
            after0(0, 0)
            chunks(act, step)
            after2(NC - 3, (NC - 3) % BUFS)
            after1(NC - 1, (NC - 1) % BUFS)
            after2(NC - 2, (NC - 2) % BUFS)
            after2(NC - 1, (NC - 1) % BUFS)

            act.wait_ge(s_ot, 2)
            nc.scalar.copy(outT[:, :, :, O:O + 1], uz[:, 0:B // P].rearrange("p (g k a) -> p g k a", k=4, a=1)
                           ).then_inc(s_otc, 1)

        @block.vector
        def _(dve):
            dve.wait_ge(s_w0, 16)
            w0v = w0raw.rearrange("o (h m) -> o h m", m=F)
            for r in range(2):
                nc.vector.tensor_tensor(doubled(0)[:, :, F * r:F * r + F], w0v, w0v.rearrange("o h m -> o m h"),
                                        ALU.add).then_inc(s_prep, 1)
            dve.wait_ge(s_prep, 2)
            nc.vector.tensor_copy(w0rot[:, :, :], rotated(0, F // 2 + 1)).then_inc(s_prep, 1)
            dve.wait_ge(s_prep, 3)
            nc.vector.tensor_scalar(w0rot[:, 0, :], w0rot[:, 0, :], 0.5, None, ALU.mult)
            nc.vector.memset(w16[:, :, :], 0.0).then_inc(s_prep, 1)
            dve.wait_ge(s_prep, 4)
            for half in range(2):
                last = nc.vector.tensor_copy(w16[:, :, P // 2 * half:P // 2 * half + G],
                                             w0rot[:, F // 2:F // 2 + 1, 0:G].broadcast_to([P, BUFS, G]))
            last.then_inc(s_wrot, 1)
            dve.wait_ge(s_w1, 16)
            for r in range(2):
                nc.vector.tensor_copy(doubled(1)[:, :, F * r:F * r + F], w1v(0)).then_inc(s_prep, 1)
            dve.wait_ge(s_prep, 6)
            dve.wait_ge(s_w1d, 2)
            for ab in range(2):
                for par in range(2):
                    last = nc.vector.tensor_copy(w1rot[:, ab, par::2, :], rotated(1 + (par + ab) % 2, F)[:, par::2, :])
            last.then_inc(s_wrot, 1)
            def layer0(c, k, i):
                dve.wait_ge(s_x[k], 16 * XDMAS * (i + 1))
                if not known(c) or c >= 1:
                    dve.wait_ge(s_z0, c)
                dve.wait_ge(s_xps, c + 1)
                nc.vector.tensor_tensor(prod0[:, :, :], xps[:, :].unsqueeze(1).broadcast_to([P, T0, C]),
                                        xlo[:, k, :, :], ALU.mult).then_inc(s_p0, 1)

            def layer1(c, k, i):
                for n in MADE:
                    ab, t0, count, _ = UNITS[n]
                    dve.wait_ge(s_h, 2 * c + ab + 1)
                    if n == [m for m in MADE if UNITS[m][1] >= T0][0]:
                        dve.wait_ge(s_xhi[k % 2], 64 * (BUFS // 2 * i + k // 2 + 1))
                    if not known(c) or c >= 1:
                        dve.wait_ge(s_lo[n], LOWS[n] * c)
                    nc.vector.tensor_tensor(prod1[:, tiles(n), :],
                                            h1[ab][k % 2][:, :].unsqueeze(1).broadcast_to([P, count, C]),
                                            rotated_x(k, t0, count), ALU.mult).then_inc(s_p1[n], 1)
                for n in range(NU):
                    if UNITS[n][3] == "dve":
                        dve.wait_ge(s_hi[n], len(parts(n)) * (c + 1))
                        low_half(nc.vector, tiles(n)).then_inc(s_lo[n], 1)

            def layer2(c, k, i):
                dve.wait_ge(s_u, c + 1)
                dve.wait_ge(s_xq[k % 2], 32 * (BUFS // 2 * i + k // 2 + 1))
                if not known(c) or c >= 1:
                    dve.wait_ge(s_zT, c)
                nc.vector.tensor_tensor(v[:, :], u, xq[:, k % 2, :], ALU.mult).then_inc(s_v, 1)

            def reduce(c, k):
                dve.wait_ge(s_z1r, c + 1)
                nc.vector.tensor_reduce(sums[:, bass.ds(c * CB, CB)],
                                        direct[:, k, :].rearrange("o (b d) -> o b d", d=D), AX_X,
                                        ALU.add).then_inc(s_sum, 1)

            def step(i, k):
                c = BUFS * i + k
                more = k == BUFS - 2 and (not known(c) or c + BUFS < NC)
                if not known(c) or c + 1 < NC:
                    layer0(c + 1, (k + 1) % BUFS, i + (k + 1) // BUFS)
                if more:
                    product16(i + 1)
                layer1(c, k, i)
                if more:
                    low16(i + 1)
                if not known(c) or c >= 2:
                    layer2(c - 2, (k - 2) % BUFS, i + (k - 2) // BUFS)
                    reduce(c - 2, (k - 2) % BUFS)

            def product16(g):
                dve.wait_ge(s_x16, 64 * (g + 1))
                nc.vector.tensor_tensor(prod16[:, :], xa[:, :], xb[:, :], ALU.mult).then_inc(s_p16, 1)

            def low16(g):
                dve.wait_ge(s_h16, g + 1)
                half = slice(P // 2, P)
                nc.vector.tensor_tensor(prod16r[half, :], prod16[half, :], prod16r[half, :].bitcast(F32),
                                        ALU.subtract).then_inc(s_l16, 1)

            dve.wait_ge(s_trc, 2)
            nc.vector.tensor_tensor(w16l[:, :, :], z1_tiles(1, 0, BUFS), w16h[:, :, :].bitcast(F32),
                                    ALU.subtract).then_inc(s_wl, 1)
            layer0(0, 0, 0)
            for g in range(GROUPS):
                dve.wait_ge(s_trc, g + 3)
                nc.vector.tensor_tensor(w1Tl[:, 4 * g:4 * g + 4, :], z1_tiles(g, 0, 4),
                                        w1Th[:, 4 * g:4 * g + 4, :].bitcast(F32), ALU.subtract).then_inc(s_wl, 1)
            product16(0)
            low16(0)
            chunks(dve, step)
            for c in range(NC - 2, NC):
                layer2(c, c % BUFS, c // BUFS)
                reduce(c, c % BUFS)

            dve.wait_ge(s_ot, 1)
            for g, bank in enumerate([z1[0], z1[1], h1[0][0], h1[0][1]]):
                last = nc.vector.tensor_copy(outT[:, g, :, 0:O], bank[:, :].rearrange("p (k o) -> p k o", k=4))
            last.then_inc(s_otc, 1)


_INS = ['r_x', 'L0_rec_W0', 'L0_rec_b0', 'L0_rec_W1', 'L0_rec_b1', 'L0_rec_W2', 'L0_rec_b2']


def kernel(**inputs):
    import numpy as _np
    import concourse.bacc as _bacc
    from concourse import mybir as _mybir
    from concourse.bass_utils import run_bass_kernel_spmd as _run

    nc = _bacc.Bacc("TRN2", target_bir_lowering=False, num_devices=1)
    arrays, args = {}, []
    for name in _INS:
        a = _np.ascontiguousarray(inputs[name])
        arrays[f"in_{name}_dram"] = a
        args.append(nc.dram_tensor(f"in_{name}_dram", a.shape, _mybir.dt.from_np(a.dtype), kind="ExternalInput").ap())
    shape = (inputs['r_x'].shape[0], inputs['L0_rec_W0'].shape[0] + 1)
    args.append(nc.dram_tensor("out_0_dram", shape, _mybir.dt.float32, kind="ExternalOutput").ap())
    cin_kernel(nc, *args)
    r = _run(nc, [arrays], core_ids=[0])
    return r.results[0]["out_0_dram"]
```
